# Optimizing a Trainium2 kernel written in Bass

```python
import numpy as np
import jax
import jax.numpy as jnp

def _softmax(x, axis=-1):
    return jax.nn.softmax(x, axis=axis)

def _gelu(x):
    return jax.nn.gelu(x, approximate=True)

def _silu(x):
    return jax.nn.silu(x)

def _sigmoid(x):
    return jax.nn.sigmoid(x)

def _layernorm(x, axis=-1, eps=1e-05):
    m = jnp.mean(x, axis=axis, keepdims=True)
    v = jnp.var(x, axis=axis, keepdims=True)
    return (x - m) / jnp.sqrt(v + eps)

def _scatter_add(tgt, idx, src, axis=0):
    return tgt.at[idx].add(src)

def _segment_sum(src, seg, n):
    return jax.ops.segment_sum(src, seg, n)
kernel_name = 'mk_conv_preact_d1_conv_nhwc384_r2_3da043'

def setup_inputs(seed: int=0):
    np.random.seed(seed)
    _w = jnp.asarray

    def _rec_inputs():
        import jax
        import jax.numpy as jnp
        _gk = jax.random.key(seed)
        x = 0.0001064 + 1 * jax.random.normal(jax.random.fold_in(_gk, 1), (2, 128, 128, 192), jnp.float32)
        return x
    x = _rec_inputs()

    def _L0_conv_setup():
        import jax, jax.numpy as jnp
        import numpy as np
        WINDOW = (1, 5, 20)
        FILL = 1.0

        def box_sum(x, axis, w):
            if w == 1:
                return x
            lo = w // 2
            hi = w - lo - 1
            xm = jnp.moveaxis(x, axis, -1)
            shp = xm.shape
            xr = xm.reshape(-1, 1, shp[-1])
            k = jnp.ones((1, 1, w), x.dtype)
            y = jax.lax.conv_general_dilated(xr, k, window_strides=(1,), padding=[(lo, hi)])
            return jnp.moveaxis(y.reshape(shp), -1, axis)
        key = jax.random.key(seed)
        x = jax.random.normal(key, (2, 128, 128, 192), dtype=jnp.float32)
        return {'x': x}
    _L0_conv_all = _L0_conv_setup()
    _L0_conv_in = {k: v for k, v in _L0_conv_all.items() if k in ()}
    del _L0_conv_all
    return {'x': x}

def reference(x):
    import jax
    import jax.numpy as jnp

    def _L0_conv_ref(x):
        import jax, jax.numpy as jnp
        import numpy as np
        WINDOW = (1, 5, 20)
        FILL = 1.0

        def box_sum(x, axis, w):
            if w == 1:
                return x
            lo = w // 2
            hi = w - lo - 1
            xm = jnp.moveaxis(x, axis, -1)
            shp = xm.shape
            xr = xm.reshape(-1, 1, shp[-1])
            k = jnp.ones((1, 1, w), x.dtype)
            y = jax.lax.conv_general_dilated(xr, k, window_strides=(1,), padding=[(lo, hi)])
            return jnp.moveaxis(y.reshape(shp), -1, axis)
        w0, w1, w2 = WINDOW
        s = box_sum(box_sum(x, 1, w0), 2, w1)
        num = box_sum(s * s, 3, w2)
        d = box_sum(box_sum(box_sum(x * x, 1, w0), 2, w1), 3, w2)
        c0 = box_sum(jnp.ones((x.shape[1],), x.dtype), 0, w0)
        c1 = box_sum(jnp.ones((x.shape[2],), x.dtype), 0, w1)
        norm = c0[:, None] * c1[None, :]
        denum = d * norm[None, :, :, None]
        return jnp.nan_to_num(num / denum, nan=FILL)

    def _gn(v, G=32, eps=1e-05):
        B_, H_, W_, C_ = v.shape
        g = v.reshape(B_, H_, W_, G, C_ // G)
        m = jnp.mean(g, axis=(1, 2, 4), keepdims=True)
        s = jnp.var(g, axis=(1, 2, 4), keepdims=True)
        return ((g - m) / jnp.sqrt(s + eps)).reshape(v.shape)

    def _ln_c(v, eps=1e-06):
        m = jnp.mean(v, axis=-1, keepdims=True)
        s = jnp.var(v, axis=-1, keepdims=True)
        return (v - m) / jnp.sqrt(s + eps)

    def _ln_t(v, eps=1e-05):
        m = jnp.mean(v, axis=-1, keepdims=True)
        s = jnp.var(v, axis=-1, keepdims=True)
        return (v - m) / jnp.sqrt(s + eps)

    def _to_tokens(v):
        B_, H_, W_, C_ = v.shape
        return v.reshape(B_, H_ * W_, C_)

    def _from_tokens(t, like):
        return t.reshape(like.shape)
    x = x + _L0_conv_ref(_gn(x))
    return x

_drawn_inputs = setup_inputs


def setup_inputs(seed=0):
    import zlib

    import numpy as np

    out = dict(_drawn_inputs(seed))
    spreads = {}
    factors = {}
    for name, (base, spread) in spreads.items():
        noise = np.random.default_rng([zlib.crc32(name.encode()), seed]).standard_normal(out[name].shape)
        drawn = base * np.exp(spread * noise) if base else spread * noise
        out[name] = jnp.asarray(drawn.astype(out[name].dtype))
    for name, factor in factors.items():
        out[name] = (out[name] * factor).astype(out[name].dtype)
    return out
```

```python
from contextlib import ExitStack

import concourse.bass as bass
from concourse import mybir

F32 = mybir.dt.float32
ALU = mybir.AluOpType
ACT = mybir.ActivationFunctionType
AX = mybir.AxisListType

BATCH, ROWS, W, C = 2, 128, 128, 192
GROUPS = 32
GC = C // GROUPS
W_WIN, C_WIN = 5, 20
W_LO = W_WIN // 2
C_LO = C_WIN // 2
C_HI = C_WIN - C_LO - 1
EPS = 1e-5
TINY = 1e-26

CA = 128
CB = C - CA
NA = CA + C_LO
B0 = CA - C_HI - 1
NB = C - B0

PAIR = 2
STEP = 8
PPS = STEP // PAIR
STEPS = ROWS // STEP
TOTAL = BATCH * STEPS
PCOLS = PAIR * C
TILES = PCOLS // 128
QUAD = 2

SLOTS = 24
HOME = (8, 0)
CHUNK = 32
CHUNKS = ROWS // CHUNK
SPC = CHUNK // STEP
STATS_STEPS = 3
SHARES = ((0, 11), (11, 22), (22, 32))
COEF_STEP = CHUNKS * STATS_STEPS
HALF_COUNT = CHUNK * GC // 2
TRIPLES = 2 * CHUNKS


def static(v):
    return isinstance(v, int)


def wait_count(eng, sem, count):
    if not static(count) or count > 0:
        eng.wait_ge(sem, count)


def window_ratio_kernel(nc, x, out):
    ctx = ExitStack()
    with ctx:
        sb = lambda name, shape: ctx.enter_context(nc.sbuf_tensor(name, shape, F32))
        ps = lambda name: ctx.enter_context(nc.psum_tensor(name, [128, 512], F32))
        sem = lambda name: ctx.enter_context(nc.semaphore(name))

        xs = sb("xs", [128, SLOTS * STEP, C])
        xc = [sb(f"xc{i}", [128, PPS, PCOLS]) for i in range(2)]
        xc2 = [sb(f"xc2_{i}", [128, PPS, PCOLS]) for i in range(2)]
        s2 = [sb(f"s2_{i}", [128, PCOLS]) for i in range(2)]
        u = [sb(f"u_{i}", [128, PCOLS]) for i in range(2)]
        r0 = [sb(f"r0_{i}", [128, PCOLS]) for i in range(2)]
        q = [sb(f"q_{i}", [128, PCOLS]) for i in range(2)]
        t1 = sb("t1", [128, PPS, PCOLS])
        t2 = sb("t2", [128, PPS, PCOLS])
        b5 = sb("b5", [128, W])
        b5d = sb("b5d", [128, W])
        b20a = sb("b20a", [128, NA])
        b20b = sb("b20b", [128, PAIR, NB])
        b20a_r = [sb(f"b20a_r{b}", [128, NA]) for b in range(BATCH)]
        b20b_r = [sb(f"b20b_r{b}", [128, PAIR, NB]) for b in range(BATCH)]
        mean_c = [sb(f"mean_c{b}", [128, C]) for b in range(BATCH)]
        averager = sb("averager", [128, 128])
        tiny_bias = sb("tiny_bias", [128, 1])
        triples = sb("triples", [128, GROUPS, TRIPLES, 3])
        dev = sb("dev", [128, GROUPS, TRIPLES])
        mean_sum = sb("mean_sum", [128, GROUPS])
        dev_sum = sb("dev_sum", [128, GROUPS])
        m2_sum = sb("m2_sum", [128, GROUPS])
        ssq_c = sb("ssq_c", [128, CA + 2 * CB])
        inv_var = sb("inv_var", [128, 2])

        S = [ps("S0"), ps("S1")]
        U = [ps("U0"), ps("U1")]
        D = [ps("D0"), ps("D1")]
        N = [ps("N0"), ps("N1")]
        mean_ps = D[0][:, PCOLS:PCOLS + GROUPS]
        var_ps = D[1][:, PCOLS:PCOLS + 2]

        loaded = [[sem(f"loaded{b}_{j}") for j in range(CHUNKS)] for b in range(BATCH)]
        consts_ready = sem("consts_ready")
        pool_own = sem("pool_own")
        dve_own = sem("dve_own")
        mean_sum_ready = sem("mean_sum_ready")
        mean_in_psum = sem("mean_in_psum")
        ssq_ready = sem("ssq_ready")
        var_in_psum = sem("var_in_psum")
        mean_ready = sem("mean_ready")
        b20_ready = sem("b20_ready")
        xc_ready = sem("xc_ready")
        xc2_ready = sem("xc2_ready")
        s_ready = sem("s_ready")
        u_ready = sem("u_ready")
        s2_ready = sem("s2_ready")
        us_ready = sem("us_ready")
        d_ready = sem("d_ready")
        n_ready = sem("n_ready")
        r0_ready = sem("r0_ready")
        q_ready = sem("q_ready")
        t1_ready = sem("t1_ready")
        t2_ready = sem("t2_ready")
        ratio_ready = sem("ratio_ready")
        out_ready = sem("out_ready")
        stored = [sem("stored0"), sem("stored1")]

        block = ctx.enter_context(nc.Block())

        def x_rows(step, b, first=0, count=STEP):
            at = (step - b * STEPS + HOME[b]) * STEP + first
            return xs[:, bass.ds(at, count), :]

        def dram_rows(t, b, step, count):
            return t[b, bass.ds((step - b * STEPS) * STEP, count * STEP), :, :].rearrange("h w c -> w h c")

        def load_second_half(sp, t):
            sp.wait_ge(stored[t % 2], 16 * (t // 2 + 1))
            at = (HOME[0] + t) * STEP
            sp.dma_start(xs[:, at:at + STEP, :], dram_rows(x, 1, STEPS + STEPS // 2 + t, 1))\
              .then_inc(loaded[1][CHUNKS // 2 + t // SPC], 16)

        @block.sync
        def _(sp):
            for j in range(CHUNKS):
                sp.dma_start(xs[:, (HOME[0] + j * SPC) * STEP:(HOME[0] + (j + 1) * SPC) * STEP, :],
                             dram_rows(x, 0, j * SPC, SPC)).then_inc(loaded[0][j], 16)
            for j in range(CHUNKS // 2):
                sp.dma_start(xs[:, (HOME[1] + j * SPC) * STEP:(HOME[1] + (j + 1) * SPC) * STEP, :],
                             dram_rows(x, 1, STEPS + j * SPC, SPC)).then_inc(loaded[1][j], 16)

            def store(t, b, parity):
                sp.wait_ge(out_ready, (PPS // QUAD) * (t + 1))
                sp.dma_start(dram_rows(out, b, t, 1), x_rows(t, b)).then_inc(stored[parity], 16)

            reused = STEPS // 2
            for t in range(reused):
                store(t, 0, t % 2)
                if t:
                    load_second_half(sp, t - 1)
            store(reused, 0, 0)
            load_second_half(sp, reused - 1)
            store(reused + 1, 0, 1)
            with sp.Fori(reused // 2 + 1, STEPS // 2) as i:
                store(2 * i, 0, 0)
                store(2 * i + 1, 0, 1)
            with sp.Fori(STEPS // 2, STEPS) as i:
                store(2 * i, 1, 0)
                store(2 * i + 1, 1, 1)
            for parity in range(2):
                sp.wait_ge(stored[parity], 16 * TOTAL // 2)

        def wait_loaded(eng, b, chunk):
            eng.wait_ge(loaded[b][chunk], 16 * SPC if b and chunk >= CHUNKS // 2 else 16)

        @block.gpsimd
        def _(pool):
            own = [0]

            def band(ap, conditions):
                nc.gpsimd.memset(ap, 1.0).then_inc(pool_own, 1)
                own[0] += 1
                for base, channel, pattern in conditions:
                    pool.wait_ge(pool_own, own[0])
                    nc.gpsimd.affine_select(out=ap, in_=ap, compare_op=ALU.is_ge, fill=0.0, base=base,
                                            pattern=pattern, channel_multiplier=channel)\
                      .then_inc(pool_own, 1)
                    own[0] += 1

            band(b5[:, :], [(W_LO, -1, [[1, W]]), (W_LO, 1, [[-1, W]])])
            band(b20a[:, :], [(C_HI, -1, [[1, NA]]), (C_LO, 1, [[-1, NA]])])
            band(b20b[:, :, :], [
                (B0 - CA + C_HI, -1, [[CB, PAIR], [1, NB]]), (CA - B0 + C_LO, 1, [[-CB, PAIR], [-1, NB]]),
                (0, 1, [[-CB, PAIR], [0, NB]]), (CB - 1, -1, [[CB, PAIR], [0, NB]])])
            pool.wait_ge(pool_own, own[0])
            nc.gpsimd.memset(averager[:, :], 1.0 / (TRIPLES * 128)).then_inc(consts_ready, 1)

            def centre(t, b, buf):
                wait_count(pool, s_ready, PPS * (t - 1))
                wait_count(pool, xc2_ready, t - 1)
                rows = x_rows(t, b).rearrange("p (n r) c -> p n r c", r=PAIR)
                for c0, c1 in ((0, CA), (CA, C)):
                    to = xc[buf][:, :, PAIR * c0:PAIR * c1].rearrange("p n (r c) -> p n r c", r=PAIR)
                    mean = mean_c[b][:, c0:c1].unsqueeze(1).unsqueeze(1).to_broadcast([128, PPS, PAIR, c1 - c0])
                    last = nc.gpsimd.tensor_tensor(to, rows[:, :, :, c0:c1], mean, ALU.subtract)
                last.then_inc(xc_ready, 1)

            for b in range(BATCH):
                for j in range(CHUNKS):
                    wait_loaded(pool, b, j)
                pool.wait_ge(mean_ready, b + 1)
                if b == 0:
                    centre(0, b, 0)
                    centre(1, b, 1)
                with pool.Fori(b * STEPS // 2 + (b == 0), (b + 1) * STEPS // 2) as i:
                    centre(2 * i, b, 0)
                    centre(2 * i + 1, b, 1)

        @block.scalar
        def _(act):
            def square_xc(t, buf):
                act.wait_ge(xc_ready, t + 1)
                wait_count(act, u_ready, PPS * (t - 1))
                nc.scalar.activation(xc2[buf][:, :, :], xc[buf][:, :, :], ACT.Square).then_inc(xc2_ready, 1)

            def first_stage(n, k):
                act.wait_ge(s_ready, n + 1)
                wait_count(act, n_ready, n - 1)
                nc.scalar.activation(s2[k % 2][:, :], S[k % 2][:, 0:PCOLS], ACT.Square).then_inc(s2_ready, 1)
                act.wait_ge(u_ready, n + 1)
                wait_count(act, d_ready, n - 1)
                nc.scalar.activation(u[k % 2][:, :], U[k % 2][:, 0:PCOLS], ACT.Copy).then_inc(us_ready, 1)

            def invert(n, k):
                act.wait_ge(d_ready, n + 1)
                wait_count(act, q_ready, n - 1)
                nc.scalar.activation(r0[k % 2][:, :], D[k % 2][:, 0:PCOLS], ACT.Abs_reciprocal_sqrt,
                                     bias=tiny_bias[:, 0:1]).then_inc(r0_ready, 1)
                act.wait_ge(r0_ready, n + 1)
                wait_count(act, t2_ready, n - 1)
                nc.scalar.activation(q[k % 2][:, :], r0[k % 2][:, :], ACT.Square).then_inc(q_ready, 1)

            def two_steps(i, last=False):
                for k in range(2 * PPS):
                    n = 2 * PPS * i + k
                    if not (last and k == 2 * PPS - 1):
                        first_stage(n + 1, k + 1)
                    invert(n, k)
                    if k % PPS == 1 and not (last and k > PPS):
                        square_xc(2 * i + k // PPS + 1, (k // PPS + 1) % 2)

            act.wait_ge(consts_ready, 2)
            square_xc(0, 0)
            first_stage(0, 0)
            two_steps(0)
            with act.Fori(1, TOTAL // 2 - 1) as i:
                two_steps(i)
            two_steps(TOTAL // 2 - 1, last=True)

        @block.tensor
        def _(pe):
            def first_stage(n, t, k):
                pair, buf = k % PPS, (k // PPS) % 2
                tiles = lambda a: [a[buf][:, pair, 128 * j:128 * (j + 1)] for j in range(TILES)]
                if k % PPS == 0:
                    pe.wait_ge(xc_ready, t + 1)
                wait_count(pe, s2_ready, n - 1)
                for j, tile in enumerate(tiles(xc)):
                    mm = nc.tensor.matmul(S[k % 2][:, 128 * j:128 * (j + 1)], tile, b5[:, :], start=True, stop=True)
                mm.then_inc(s_ready, 1)
                if k % PPS == 0:
                    pe.wait_ge(xc2_ready, t + 1)
                wait_count(pe, us_ready, n - 1)
                for j, tile in enumerate(tiles(xc2)):
                    mm = nc.tensor.matmul(U[k % 2][:, 128 * j:128 * (j + 1)], tile, b5d[:, :], start=True, stop=True)
                mm.then_inc(u_ready, 1)

            def box20(bank, data, b):
                o = bank[:, 0:PCOLS].rearrange("p (r c) -> p r c", r=PAIR)
                nc.tensor.matmul(o[:, 0, 0:NA], data[:, 0:128], b20a_r[b][:, :], start=True, stop=False,
                                 skip_group_check=True)
                nc.tensor.matmul(o[:, 1, 0:NA], data[:, 128:256], b20a_r[b][:, :], start=False, stop=False,
                                 skip_group_check=True)
                return nc.tensor.matmul(o[:, :, B0:C], data[:, 256:384], b20b_r[b][:, :, :], start=False, stop=True,
                                        skip_group_check=True)

            def second_stage(n, k, b, extra=None):
                pe.wait_ge(us_ready, n + 1)
                wait_count(pe, t1_ready, n - 1)
                mm = box20(D[k % 2], u[k % 2], b)
                if extra is not None:
                    mm = extra()
                mm.then_inc(d_ready, 1)
                pe.wait_ge(s2_ready, n + 1)
                wait_count(pe, t2_ready, n - 1)
                box20(N[k % 2], s2[k % 2], b).then_inc(n_ready, 1)

            def average_means(b):
                pe.wait_ge(mean_sum_ready, b + 1)
                return nc.tensor.matmul(mean_ps, averager[:, :], mean_sum[:, :], start=True, stop=True)

            def average_squares(b):
                pe.wait_ge(ssq_ready, b + 1)
                nc.tensor.matmul(var_ps[:, 0:1], ssq_c[:, 0:CA], averager[:, 0:1], start=True, stop=True)
                return nc.tensor.matmul(var_ps[:, 1:2], ssq_c[:, CA:CA + 2 * CB], averager[:, 0:1],
                                        start=True, stop=True)

            def two_steps(i, b, last=False, extras=None):
                for k in range(2 * PPS):
                    n = 2 * PPS * i + k
                    if not (last and k == 2 * PPS - 1):
                        first_stage(n + 1, 2 * i + (k + 1) // PPS, k + 1)
                    second_stage(n, k, b, (extras or {}).get(k))

            pe.wait_ge(consts_ready, 2)
            average_means(0).then_inc(mean_in_psum, 1)
            average_squares(0).then_inc(var_in_psum, 1)
            first_stage(0, 0, 0)
            pe.wait_ge(b20_ready, 1)
            two_steps(0, 0)
            with pe.Fori(1, COEF_STEP // 2) as i:
                two_steps(i, 0)
            two_steps(COEF_STEP // 2, 0, extras={0: lambda: average_means(1), 7: lambda: average_squares(1)})
            two_steps(COEF_STEP // 2 + 1, 0)
            pe.wait_ge(b20_ready, 2)
            with pe.Fori(STEPS // 2, TOTAL // 2 - 1) as i:
                two_steps(i, 1)
            two_steps(TOTAL // 2 - 1, 1, last=True)

        @block.vector
        def _(dve):
            own = [0]

            def link(ins):
                own[0] += 1
                ins.then_inc(dve_own, 1)
                dve.wait_ge(dve_own, own[0])

            def measure(b, chunk, g0, g1):
                for g in range(g0, g1):
                    rows = xs[:, bass.ds((HOME[b] + SPC * chunk) * STEP, CHUNK), g * GC:(g + 1) * GC]
                    to = triples[:, g, bass.ds(2 * chunk, 2), :].rearrange("p a b -> p (a b)")
                    last = nc.vector.bn_stats(to, rows)
                return last

            def sum_means():
                nc.vector.tensor_reduce(mean_sum[:, :], triples[:, :, :, 1], AX.X, ALU.add).then_inc(mean_sum_ready, 1)

            def spread_mean(b):
                mean_g = mean_ps.unsqueeze(2)
                nc.vector.tensor_copy(mean_c[b][:, :].rearrange("p (g c) -> p g c", g=GROUPS),
                                      mean_g.to_broadcast([128, GROUPS, GC])).then_inc(mean_ready, 1)
                link(nc.vector.tensor_tensor(dev[:, :, :], triples[:, :, :, 1],
                                             mean_g.to_broadcast([128, GROUPS, TRIPLES]), ALU.subtract))

            def sum_squares():
                link(nc.vector.tensor_tensor(dev[:, :, :], dev[:, :, :], dev[:, :, :], ALU.mult))
                link(nc.vector.tensor_reduce(dev_sum[:, :], dev[:, :, :], AX.X, ALU.add))
                link(nc.vector.tensor_reduce(m2_sum[:, :], triples[:, :, :, 2], AX.X, ALU.add))
                link(nc.vector.scalar_tensor_tensor(m2_sum[:, :], dev_sum[:, :], float(HALF_COUNT), m2_sum[:, :],
                                                    ALU.mult, ALU.add))
                link(nc.vector.tensor_copy(ssq_c[:, 0:C].rearrange("p (g c) -> p g c", g=GROUPS),
                                           m2_sum[:, :].unsqueeze(2).to_broadcast([128, GROUPS, GC])))
                nc.vector.tensor_copy(ssq_c[:, C:C + CB], ssq_c[:, CA:C]).then_inc(ssq_ready, 1)

            def fold_variance(b):
                link(nc.vector.tensor_scalar(inv_var[:, :], var_ps, 1.0 / HALF_COUNT, EPS, ALU.mult, ALU.add))
                link(nc.vector.reciprocal(inv_var[:, :], inv_var[:, :]))
                nc.vector.tensor_scalar(b20a_r[b][:, :], b20a[:, :], inv_var[:, 0:1], None, ALU.mult)
                nc.vector.tensor_scalar(b20b_r[b][:, :, :], b20b[:, :, :], inv_var[:, 1:2], None, ALU.mult)\
                  .then_inc(b20_ready, 1)

            def quotient(n, k):
                dve.wait_ge(q_ready, n + 1)
                nc.vector.scalar_tensor_tensor(t1[:, k, :], D[k % 2][:, 0:PCOLS], -TINY, q[k % 2][:, :],
                                               ALU.add, ALU.mult).then_inc(t1_ready, 1)
                dve.wait_ge(n_ready, n + 1)
                nc.vector.scalar_tensor_tensor(t2[:, k, :], N[k % 2][:, 0:PCOLS], TINY, q[k % 2][:, :],
                                               ALU.add, ALU.mult).then_inc(t2_ready, 1)

            def finish(t, n, k, b):
                f = lambda a: a[:, k - QUAD + 1:k + 1, :].rearrange("p a b -> p (a b)")
                rows = x_rows(t, b, PAIR * (k - QUAD + 1), PAIR * QUAD).rearrange("p a b -> p (a b)")
                dve.wait_ge(t2_ready, n + 1)
                nc.vector.scalar_tensor_tensor(f(t1), f(t1), 2.0, f(t2), ALU.add, ALU.mult)\
                  .then_inc(ratio_ready, 1)
                dve.wait_ge(ratio_ready, (PPS // QUAD) * t + k // QUAD + 1)
                nc.vector.scalar_tensor_tensor(rows, f(t1), 1.0, rows, ALU.min, ALU.add).then_inc(out_ready, 1)

            def step(t, b, before=None):
                for k in range(PPS):
                    n = PPS * t + k
                    if before and k in before:
                        before[k]()
                    quotient(n, k)
                    if k % QUAD == QUAD - 1:
                        finish(t, n, k, b)

            nc.vector.memset(tiny_bias[:, :], -TINY)
            dve.wait_ge(consts_ready, 1)
            link(nc.vector.tensor_scalar(b5d[:, :], b5[:, :], -float(W_WIN), None, ALU.mult))
            for e in range(W_LO):
                for w in (e, W - 1 - e):
                    last = nc.vector.tensor_scalar(b5d[:, w:w + 1], b5[:, w:w + 1], -float(W_LO + 1 + e), None,
                                                   ALU.mult)
            last.then_inc(consts_ready, 1)

            for j in range(CHUNKS):
                wait_loaded(dve, 0, j)
                last = measure(0, j, 0, GROUPS)
            link(last)
            sum_means()
            dve.wait_ge(mean_in_psum, 1)
            spread_mean(0)
            sum_squares()
            dve.wait_ge(var_in_psum, 1)
            fold_variance(0)

            for j in range(CHUNKS):
                wait_loaded(dve, 1, j)
                for s, (g0, g1) in enumerate(SHARES):
                    step(STATS_STEPS * j + s, 0)
                    last = measure(1, j, g0, g1)
            link(last)
            sum_means()

            def take_mean():
                dve.wait_ge(q_ready, PPS * COEF_STEP + 1)
                spread_mean(1)

            step(COEF_STEP, 0, before={0: take_mean})
            sum_squares()

            def take_variance():
                dve.wait_ge(q_ready, PPS * (COEF_STEP + 2))
                fold_variance(1)

            step(COEF_STEP + 1, 0, before={PPS - 1: take_variance})
            with dve.Fori(COEF_STEP + 2, STEPS) as t:
                step(t, 0)
            with dve.Fori(STEPS, TOTAL) as t:
                step(t, 1)


def kernel(x):
    import numpy as np
    import concourse.bacc as bacc
    from concourse.bass_utils import run_bass_kernel_spmd

    nc = bacc.Bacc("TRN2", target_bir_lowering=False, num_devices=1)
    x = np.ascontiguousarray(x)
    x_dram = nc.dram_tensor("x", x.shape, F32, kind="ExternalInput").ap()
    out_dram = nc.dram_tensor("out", x.shape, F32, kind="ExternalOutput").ap()
    window_ratio_kernel(nc, x_dram, out_dram)
    r = run_bass_kernel_spmd(nc, [{"x": x}], core_ids=[0])
    return r.results[0]["out"]
```

```python
from contextlib import ExitStack

import concourse.bass as bass
from concourse import mybir

F32 = mybir.dt.float32
ALU = mybir.AluOpType
ACT = mybir.ActivationFunctionType
AX = mybir.AxisListType

BATCH, ROWS, W, C = 2, 128, 128, 192
GROUPS = 32
GC = C // GROUPS
W_WIN, C_WIN = 5, 20
W_LO = W_WIN // 2
C_LO = C_WIN // 2
C_HI = C_WIN - C_LO - 1
EPS = 1e-5
TINY = 1e-26

CA = 128
CB = C - CA
NA = CA + C_LO
B0 = CA - C_HI - 1
NB = C - B0

PAIR = 2
STEP = 8
PPS = STEP // PAIR
STEPS = ROWS // STEP
TOTAL = BATCH * STEPS
PAIRS = STEPS * PPS
PCOLS = PAIR * C
TILES = PCOLS // 128
QUAD = 2
RING = 4
LEAD = 3

RAW = 10
SLOTS = RAW + STEPS
HOME = (RAW, 0)
LOADS = 8
LOAD_STEPS = STEPS // LOADS

BLOCK = 32
BLOCKS = ROWS // BLOCK
SPB = BLOCK // STEP
LATE_SETS = ((0, 3), (1, 2))
TRIPLES = (2 * BLOCKS, 2 * len(LATE_SETS))
COUNT = tuple(ROWS * GC // n for n in TRIPLES)
STATS_FROM = 7
STATS_STEPS = 4
MEAN_AT, VAR_AT = (STEPS - 1, 1), (STEPS - 1, 3)


def static(v):
    return isinstance(v, int)


def wait_count(eng, sem, count):
    if not static(count) or count > 0:
        eng.wait_ge(sem, count)


def window_ratio_kernel(nc, x, out):
    ctx = ExitStack()
    with ctx:
        sb = lambda name, shape: ctx.enter_context(nc.sbuf_tensor(name, shape, F32))
        ps = lambda name: ctx.enter_context(nc.psum_tensor(name, [128, 512], F32))
        sem = lambda name: ctx.enter_context(nc.semaphore(name))

        xs = sb("xs", [128, SLOTS * STEP, C])
        xc = sb("xc", [128, RING, PCOLS])
        xc2 = sb("xc2", [128, RING, PCOLS])
        s2 = [sb(f"s2_{i}", [128, PCOLS]) for i in range(2)]
        u = [sb(f"u_{i}", [128, PCOLS]) for i in range(2)]
        q = [sb(f"q_{i}", [128, PCOLS]) for i in range(2)]
        t1 = sb("t1", [128, PPS, PCOLS])
        t2 = sb("t2", [128, QUAD, PCOLS])
        b5 = sb("b5", [128, W])
        b5d = sb("b5d", [128, W])
        b20a = sb("b20a", [128, NA])
        b20b = sb("b20b", [128, PAIR, NB])
        b20a_r = [sb(f"b20a_r{b}", [128, NA]) for b in range(BATCH)]
        b20b_r = [sb(f"b20b_r{b}", [128, PAIR, NB]) for b in range(BATCH)]
        mean_c = [sb(f"mean_c{b}", [128, C]) for b in range(BATCH)]
        averager = [sb(f"averager{b}", [128, 128]) for b in range(BATCH)]
        c1_row = sb("c1_row", [128, W])
        c1_mean = sb("c1_mean", [128, PCOLS])
        tiny_bias = sb("tiny_bias", [128, 1])
        triples = [sb(f"triples{b}", [128, GROUPS, TRIPLES[b], 3]) for b in range(BATCH)]
        dev = sb("dev", [128, GROUPS, TRIPLES[0]])
        mean_sum = sb("mean_sum", [128, GROUPS])
        dev_sum = sb("dev_sum", [128, GROUPS])
        m2_sum = sb("m2_sum", [128, GROUPS])
        ssq_c = sb("ssq_c", [128, C])
        inv_var = sb("inv_var", [128, 2])

        S = [ps("S0"), ps("S1")]
        U = [ps("U0"), ps("U1")]
        D = [ps("D0"), ps("D1")]
        N = [ps("N0"), ps("N1")]
        mean_ps = D[1][:, PCOLS:PCOLS + GROUPS]
        var_ps = D[1][:, PCOLS + GROUPS:PCOLS + GROUPS + 2]
        c1_mean_ps = N[1][:, 0:PCOLS]

        loaded0 = [sem(f"loaded0_{j}") for j in range(LOADS)]
        loaded1 = [sem(f"loaded1_{j}") for j in range(len(LATE_SETS))]
        raw_kept = sem("raw_kept")
        c1_mean_in_psum = sem("c1_mean_in_psum")
        c1_mean_ready = sem("c1_mean_ready")
        raw_centred = sem("raw_centred")
        consts_ready = sem("consts_ready")
        pool_own = sem("pool_own")
        dve_own = sem("dve_own")
        mean_sum_ready = sem("mean_sum_ready")
        mean_in_psum = sem("mean_in_psum")
        ssq_ready = sem("ssq_ready")
        var_in_psum = sem("var_in_psum")
        mean_ready = sem("mean_ready")
        b20_ready = sem("b20_ready")
        xc_ready = sem("xc_ready")
        xc2_ready = sem("xc2_ready")
        s_ready = sem("s_ready")
        u_ready = sem("u_ready")
        s2_ready = sem("s2_ready")
        us_ready = sem("us_ready")
        d_ready = sem("d_ready")
        n_ready = sem("n_ready")
        r0_ready = sem("r0_ready")
        q_ready = sem("q_ready")
        measured = sem("measured")
        t1_ready = sem("t1_ready")
        t2_ready = sem("t2_ready")
        ratio_ready = sem("ratio_ready")
        out_ready = sem("out_ready")
        stored = [sem("stored0"), sem("stored1")]

        block = ctx.enter_context(nc.Block())

        def x_rows(n, b, pairs=1):
            return xs[:, bass.ds((n - b * PAIRS) * PAIR + HOME[b] * STEP, pairs * PAIR), :]

        def dram_rows(t, b, step, count):
            return t[b, bass.ds((step - b * STEPS) * STEP, count * STEP), :, :].rearrange("h w c -> w h c")

        def raw_box(n, pairs=1):
            flat = xs[:, 0:RAW * STEP, :].rearrange("p r c -> p (r c)")
            return flat[:, bass.ds(n * PCOLS, pairs * PCOLS)]

        def centre(eng, ops, n, k, b):
            wait_count(eng, s_ready, n - RING + 1)
            wait_count(eng, xc2_ready, n - RING + 1)
            for c0, c1 in ((0, CA), (CA, C)):
                to = xc[:, k % RING, PAIR * c0:PAIR * c1].rearrange("p (r c) -> p r c", r=PAIR)
                mean = mean_c[b][:, c0:c1].unsqueeze(1).to_broadcast([128, PAIR, c1 - c0])
                last = ops.tensor_tensor(to, x_rows(n, b)[:, :, c0:c1], mean, ALU.subtract)
            last.then_inc(xc_ready, 1)

        @block.sync
        def _(sp):
            for j in range(LOADS):
                sp.dma_start(x_rows(j * LOAD_STEPS * PPS, 0, LOAD_STEPS * PPS),
                             dram_rows(x, 0, j * LOAD_STEPS, LOAD_STEPS)).then_inc(loaded0[j], 16)

            def store(t, b, parity):
                sp.wait_ge(out_ready, (PPS // QUAD) * (t + 1))
                sp.dma_start(dram_rows(out, b, t, 1), x_rows(PPS * t, b, PPS)).then_inc(stored[parity], 16)

            def load1(t):
                arrived = next(loaded1[j] for j, blocks in enumerate(LATE_SETS) if t // SPB in blocks)
                sp.dma_start(x_rows(PAIRS + PPS * t, 1, PPS), dram_rows(x, 1, STEPS + t, 1)).then_inc(arrived, 16)

            for t in range(STEPS):
                if t < RAW:
                    sp.wait_ge(s2_ready, PPS * (t + 1))
                    load1(t)
                if 0 < t <= STEPS - RAW:
                    sp.wait_ge(stored[(t - 1) % 2], 16 * ((t - 1) // 2 + 1))
                    load1(RAW + t - 1)
                store(t, 0, t % 2)
            with sp.Fori(STEPS // 2, STEPS) as i:
                store(2 * i, 1, 0)
                store(2 * i + 1, 1, 1)
            for parity in range(2):
                sp.wait_ge(stored[parity], 16 * TOTAL // 2)

        def wait_loaded1(eng, j):
            eng.wait_ge(loaded1[j], 16 * SPB * len(LATE_SETS[j]))

        @block.gpsimd
        def _(pool):
            own = [0]

            def band(ap, conditions):
                nc.gpsimd.memset(ap, 1.0).then_inc(pool_own, 1)
                own[0] += 1
                for base, channel, pattern in conditions:
                    pool.wait_ge(pool_own, own[0])
                    nc.gpsimd.affine_select(out=ap, in_=ap, compare_op=ALU.is_ge, fill=0.0, base=base,
                                            pattern=pattern, channel_multiplier=channel)\
                      .then_inc(pool_own, 1)
                    own[0] += 1

            band(b5[:, :], [(W_LO, -1, [[1, W]]), (W_LO, 1, [[-1, W]])])
            band(b20a[:, :], [(C_HI, -1, [[1, NA]]), (C_LO, 1, [[-1, NA]])])
            band(b20b[:, :, :], [
                (B0 - CA + C_HI, -1, [[CB, PAIR], [1, NB]]), (CA - B0 + C_LO, 1, [[-CB, PAIR], [-1, NB]]),
                (0, 1, [[-CB, PAIR], [0, NB]]), (CB - 1, -1, [[CB, PAIR], [0, NB]])])
            pool.wait_ge(pool_own, own[0])
            nc.gpsimd.memset(averager[1][:, :], 1.0 / (TRIPLES[1] * 128))
            nc.gpsimd.memset(averager[0][:, :], 1.0 / (TRIPLES[0] * 128)).then_inc(consts_ready, 1)

            def centre_raw(n):
                box = raw_box(n, QUAD).rearrange("p (n w) -> p n w", n=QUAD)
                nc.gpsimd.tensor_tensor(box, box, c1_mean[:, :].unsqueeze(1).to_broadcast([128, QUAD, PCOLS]),
                                        ALU.subtract).then_inc(raw_centred, 1)

            def step(t, b, raw=False):
                for k in range(0, PPS, QUAD):
                    if raw:
                        centre_raw(PPS * t + k)
                    for m in range(k + QUAD, k + 2 * QUAD):
                        centre(pool, nc.gpsimd, PPS * t + m, m, b)

            for j in range(LOADS):
                pool.wait_ge(loaded0[j], 16)
            pool.wait_ge(raw_kept, PPS * RAW)
            pool.wait_ge(mean_ready, 1)
            for n in range(QUAD):
                centre(pool, nc.gpsimd, n, n, 0)
            pool.wait_ge(c1_mean_ready, 1)
            step(0, 0, True)
            with pool.Fori(1, RAW) as t:
                step(t, 0, True)
            with pool.Fori(RAW, STEPS - 1) as t:
                step(t, 0)
            for n in (PAIRS - 2, PAIRS - 1):
                centre(pool, nc.gpsimd, n, n, 0)
            for j in range(len(LATE_SETS)):
                wait_loaded1(pool, j)
            pool.wait_ge(mean_ready, 2)
            for n in (PAIRS, PAIRS + 1):
                centre(pool, nc.gpsimd, n, n, 1)
            with pool.Fori(STEPS, TOTAL - 1) as t:
                step(t, 1)
            for n in (2 * PAIRS - 2, 2 * PAIRS - 1):
                centre(pool, nc.gpsimd, n, n, 1)

        @block.scalar
        def _(act):
            def square_xc(t, buf):
                act.wait_ge(xc_ready, t + 1)
                wait_count(act, u_ready, PPS * (t - 1))
                nc.scalar.activation(xc2[buf][:, :, :], xc[buf][:, :, :], ACT.Square).then_inc(xc2_ready, 1)

            def first_stage(t, k, raw):
                n = PPS * t + k
                if raw:
                    act.wait_ge(raw_centred, (PPS // QUAD) * t + k // QUAD + 1)
                    source = raw_box(n)
                else:
                    act.wait_ge(s_ready, n + 1)
                    source = S[k % 2][:, 0:PCOLS]
                wait_count(act, n_ready, n - 1)
                nc.scalar.activation(s2[k % 2][:, :], source, ACT.Square).then_inc(s2_ready, 1)
                act.wait_ge(u_ready, n + 1)
                wait_count(act, d_ready, n - 1)
                nc.scalar.activation(u[k % 2][:, :], U[k % 2][:, 0:PCOLS], ACT.Copy).then_inc(us_ready, 1)

            def take_root(n, k):
                act.wait_ge(d_ready, n + 1)
                wait_count(act, t2_ready, n - 1)
                nc.scalar.activation(q[k % 2][:, :], D[k % 2][:, 0:PCOLS], ACT.Abs_reciprocal_sqrt,
                                     bias=tiny_bias[:, 0:1]).then_inc(r0_ready, 1)

            def square_root(n, k):
                act.wait_ge(r0_ready, n + 1)
                nc.scalar.activation(q[k % 2][:, :], q[k % 2][:, :], ACT.Square).then_inc(q_ready, 1)

            def square_xc(n, k):
                act.wait_ge(xc_ready, n + 1)
                wait_count(act, u_ready, n - RING + 1)
                nc.scalar.activation(xc2[:, k % RING, :], xc[:, k % RING, :], ACT.Square).then_inc(xc2_ready, 1)

            def step(t, raw=False, to_raw=False, last=False, ahead=None):
                for k in range(PPS):
                    n = PPS * t + k
                    end = k == PPS - 1
                    if not (last and end):
                        first_stage(t + end, 0 if end else k + 1, to_raw if end else raw)
                    take_root(n, k)
                    for m in ahead[k] if ahead else (k + LEAD,):
                        square_xc(PPS * t + m, m)
                    square_root(n, k)

            act.wait_ge(consts_ready, 2)
            nc.scalar.activation(q[0][:, 0:1], tiny_bias[:, 0:1], ACT.Abs_reciprocal_sqrt)
            for n in range(PPS * RAW):
                act.wait_ge(s_ready, n + 1)
                nc.scalar.activation(raw_box(n), S[n % 2][:, 0:PCOLS], ACT.Copy).then_inc(raw_kept, 1)
            act.wait_ge(c1_mean_in_psum, 1)
            nc.scalar.activation(c1_mean[:, :], c1_mean_ps, ACT.Copy).then_inc(c1_mean_ready, 1)
            for n in range(LEAD):
                square_xc(n, n)
            first_stage(0, 0, True)
            step(0, True, True)
            with act.Fori(1, RAW - 1) as t:
                step(t, True, True)
            step(RAW - 1, True, False)
            with act.Fori(RAW, STEPS - 1) as t:
                step(t)
            step(STEPS - 1, ahead=((3,), (), (4,), (5, 6)))
            with act.Fori(STEPS, TOTAL - 1) as t:
                step(t)
            step(TOTAL - 1, last=True, ahead=((3,), (), (), ()))

        @block.tensor
        def _(pe):
            def box5(bank, data, k, weights):
                for j in range(TILES):
                    tile = data[:, k % RING, 128 * j:128 * (j + 1)]
                    mm = nc.tensor.matmul(bank[k % 2][:, 128 * j:128 * (j + 1)], tile, weights[:, :],
                                          start=True, stop=True)
                return mm

            def box5_raw(n):
                for r in range(PAIR):
                    row, half = (HOME[0] * STEP) + PAIR * n + r, slice(CB * r, CB * (r + 1))
                    nc.tensor.matmul(S[n % 2][:, 128 * r:128 * (r + 1)], xs[:, row, 0:CA], b5[:, :],
                                     start=True, stop=True)
                    mm = nc.tensor.matmul(S[n % 2][half, 128 * PAIR:PCOLS], xs[:, row, CA:C], b5[:, :],
                                          start=True, stop=True)
                return mm

            def first_stage(n, k, raw):
                if not raw:
                    pe.wait_ge(xc_ready, n + 1)
                    wait_count(pe, s2_ready, n - 1)
                    box5(S, xc, k, b5).then_inc(s_ready, 1)
                pe.wait_ge(xc2_ready, n + 1)
                wait_count(pe, us_ready, n - 1)
                box5(U, xc2, k, b5d).then_inc(u_ready, 1)

            def box20(bank, data, b):
                o = bank[:, 0:PCOLS].rearrange("p (r c) -> p r c", r=PAIR)
                nc.tensor.matmul(o[:, 0, 0:NA], data[:, 0:128], b20a_r[b][:, :], start=True, stop=False,
                                 skip_group_check=True)
                nc.tensor.matmul(o[:, 1, 0:NA], data[:, 128:256], b20a_r[b][:, :], start=False, stop=False,
                                 skip_group_check=True)
                return nc.tensor.matmul(o[:, :, B0:C], data[:, 256:384], b20b_r[b][:, :, :], start=False, stop=True,
                                        skip_group_check=True)

            def second_stage(n, k, b, extra=None):
                pe.wait_ge(us_ready, n + 1)
                wait_count(pe, t1_ready, n - 1)
                mm = box20(D[k % 2], u[k % 2], b)
                if extra is not None:
                    mm = extra()
                mm.then_inc(d_ready, 1)
                pe.wait_ge(s2_ready, n + 1)
                wait_count(pe, t2_ready, n - 1)
                box20(N[k % 2], s2[k % 2], b).then_inc(n_ready, 1)

            def average_means(b):
                pe.wait_ge(mean_sum_ready, b + 1)
                return nc.tensor.matmul(mean_ps, averager[b][:, :], mean_sum[:, :], start=True, stop=True)

            def average_squares(b):
                pe.wait_ge(ssq_ready, b + 1)
                column = averager[0][:, 0:1]
                nc.tensor.matmul(var_ps[:, 0:1], ssq_c[:, 0:CA], column, start=True, stop=True)
                for r in range(PAIR):
                    mm = nc.tensor.matmul(var_ps[CB * r:CB * (r + 1), 1:2], ssq_c[:, CA:C], column,
                                          start=True, stop=True)
                return mm

            def spread_c1_mean():
                for r in range(PAIR):
                    cols, half = slice(128 * r, 128 * (r + 1)), slice(CB * r, CB * (r + 1))
                    nc.tensor.matmul(c1_mean_ps[:, cols], mean_c[0][0:1, 0:CA], c1_row[0:1, :],
                                     start=True, stop=True)
                    mm = nc.tensor.matmul(c1_mean_ps[half, 128 * PAIR:PCOLS], mean_c[0][0:1, CA:C], c1_row[0:1, :],
                                          start=True, stop=True)
                return mm

            def step(t, b, raw=False, to_raw=False, last=False, extras=None):
                for k in range(PPS):
                    n = PPS * t + k
                    end = k == PPS - 1
                    if not (last and end):
                        first_stage(n + 1, k + 1, to_raw if end else raw)
                    second_stage(n, k, b, extras.get((t, k)) if extras else None)

            pe.wait_ge(consts_ready, 2)
            for n in range(PPS * RAW):
                if n % (PPS * LOAD_STEPS) == 0:
                    pe.wait_ge(loaded0[n // (PPS * LOAD_STEPS)], 16)
                wait_count(pe, raw_kept, n - 1)
                box5_raw(n).then_inc(s_ready, 1)
            average_means(0).then_inc(mean_in_psum, 1)
            pe.wait_ge(mean_ready, 1)
            spread_c1_mean().then_inc(c1_mean_in_psum, 1)
            average_squares(0).then_inc(var_in_psum, 1)
            first_stage(0, 0, True)
            pe.wait_ge(c1_mean_ready, 1)
            pe.wait_ge(b20_ready, 1)
            step(0, 0, True, True)
            with pe.Fori(1, RAW - 1) as t:
                step(t, 0, True, True)
            pe.wait_ge(raw_kept, PPS * RAW)
            step(RAW - 1, 0, True, False)
            with pe.Fori(RAW, MEAN_AT[0]) as t:
                step(t, 0)
            for t in range(MEAN_AT[0], STEPS):
                step(t, 0, extras={MEAN_AT: lambda: average_means(1), VAR_AT: lambda: average_squares(1)})
            pe.wait_ge(b20_ready, 2)
            with pe.Fori(STEPS, TOTAL - 1) as t:
                step(t, 1)
            step(TOTAL - 1, 1, last=True)

        @block.vector
        def _(dve):
            own = [0]

            def link(ins):
                own[0] += 1
                ins.then_inc(dve_own, 1)
                dve.wait_ge(dve_own, own[0])

            def measure(b, j, g0, count):
                for g in range(count):
                    home = HOME[b] * STEP
                    rows = xs[:, home:home + ROWS, bass.ds((g0 + g) * GC, GC)]\
                        .rearrange("p (a r) c -> p a r c", r=BLOCK)
                    if b:
                        first, second = LATE_SETS[j]
                        rows = rows[:, first:second + 1:second - first, :, :]
                    else:
                        rows = rows[:, j, :, :]
                    to = triples[b][:, bass.ds(g0 + g, 1), 2 * j:2 * j + 2, :]
                    last = nc.vector.bn_stats(to.rearrange("p g a b -> p (g a b)"), rows)
                return last

            def sum_triples(b):
                nc.vector.tensor_reduce(mean_sum[:, :], triples[b][:, :, :, 1], AX.X, ALU.add)\
                  .then_inc(mean_sum_ready, 1)
                nc.vector.tensor_reduce(m2_sum[:, :], triples[b][:, :, :, 2], AX.X, ALU.add)

            def spread_mean(b):
                mean_g = mean_ps.unsqueeze(2)
                nc.vector.tensor_copy(mean_c[b][:, :].rearrange("p (g c) -> p g c", g=GROUPS),
                                      mean_g.to_broadcast([128, GROUPS, GC])).then_inc(mean_ready, 1)
                link(nc.vector.tensor_tensor(dev[:, :, 0:TRIPLES[b]], triples[b][:, :, :, 1],
                                             mean_g.to_broadcast([128, GROUPS, TRIPLES[b]]), ALU.subtract))

            def sum_squares(b):
                d = dev[:, :, 0:TRIPLES[b]]
                by_channel = lambda a: a[:, :].unsqueeze(2).to_broadcast([128, GROUPS, GC])
                link(nc.vector.tensor_tensor(d, d, d, ALU.mult))
                link(nc.vector.tensor_reduce(dev_sum[:, :], d, AX.X, ALU.add))
                nc.vector.scalar_tensor_tensor(ssq_c[:, :].rearrange("p (g c) -> p g c", g=GROUPS),
                                               by_channel(dev_sum), float(COUNT[b]), by_channel(m2_sum),
                                               ALU.mult, ALU.add).then_inc(ssq_ready, 1)

            def fold_variance(b):
                link(nc.vector.tensor_scalar(inv_var[:, :], var_ps, 1.0 / COUNT[0], EPS, ALU.mult, ALU.add))
                link(nc.vector.reciprocal(inv_var[:, :], inv_var[:, :]))
                nc.vector.tensor_scalar(b20a_r[b][:, :], b20a[:, :], inv_var[:, 0:1], None, ALU.mult)
                nc.vector.tensor_scalar(b20b_r[b][:, :, :], b20b[:, :, :], inv_var[:, 1:2], None, ALU.mult)\
                  .then_inc(b20_ready, 1)

            def quotient(n, k):
                dve.wait_ge(q_ready, n + 1)
                nc.vector.scalar_tensor_tensor(t1[:, k, :], D[k % 2][:, 0:PCOLS], -TINY, q[k % 2][:, :],
                                               ALU.add, ALU.mult).then_inc(t1_ready, 1)
                dve.wait_ge(n_ready, n + 1)
                nc.vector.scalar_tensor_tensor(t2[:, k % QUAD, :], N[k % 2][:, 0:PCOLS], TINY, q[k % 2][:, :],
                                               ALU.add, ALU.mult).then_inc(t2_ready, 1)

            def finish(t, n, k, b):
                flat = lambda a: a.rearrange("p a b -> p (a b)")
                ratio = flat(t1[:, k - QUAD + 1:k + 1, :])
                rows = flat(x_rows(n - QUAD + 1, b, QUAD))
                dve.wait_ge(t2_ready, n + 1)
                nc.vector.scalar_tensor_tensor(ratio, ratio, 2.0, flat(t2[:, :, :]), ALU.add, ALU.mult)\
                  .then_inc(ratio_ready, 1)
                dve.wait_ge(ratio_ready, (PPS // QUAD) * t + k // QUAD + 1)
                nc.vector.scalar_tensor_tensor(rows, ratio, 1.0, rows, ALU.min, ALU.add).then_inc(out_ready, 1)

            def step(t, b, before=None, after=None):
                for k in range(PPS):
                    n = PPS * t + k
                    if before and (t, k) in before:
                        before[t, k]()
                    quotient(n, k)
                    if after:
                        after(k)
                    if k % QUAD == QUAD - 1:
                        finish(t, n, k, b)

            nc.vector.memset(tiny_bias[:, :], -TINY)
            link(nc.vector.memset(c1_row[:, :], float(W_WIN)))
            for e in range(W_LO):
                for w in (e, W - 1 - e):
                    last = nc.vector.memset(c1_row[:, w:w + 1], float(W_LO + 1 + e))
            link(last)
            dve.wait_ge(consts_ready, 1)
            nc.vector.scalar_tensor_tensor(b5d[:, :], b5[:, :], -1.0, c1_row[:, :], ALU.mult, ALU.mult)\
              .then_inc(consts_ready, 1)

            for j in range(BLOCKS):
                for load in range(j * LOADS // BLOCKS, (j + 1) * LOADS // BLOCKS):
                    dve.wait_ge(loaded0[load], 16)
                last = measure(0, j, 0, GROUPS)
            link(last)
            sum_triples(0)
            dve.wait_ge(mean_in_psum, 1)
            spread_mean(0)
            sum_squares(0)
            dve.wait_ge(var_in_psum, 1)
            fold_variance(0)

            with dve.Fori(0, STATS_FROM) as t:
                step(t, 0)
            share = GROUPS // (STATS_STEPS * PPS)
            for j in range(len(LATE_SETS)):
                wait_loaded1(dve, j)
                with dve.Fori(0, STATS_STEPS) as s:
                    step(STATS_FROM + STATS_STEPS * j + s, 0,
                         after=lambda k: measure(1, j, share * (PPS * s + k), share).then_inc(measured, 1))
            dve.wait_ge(measured, len(LATE_SETS) * STATS_STEPS * PPS)
            sum_triples(1)

            def take_mean():
                dve.wait_ge(r0_ready, PPS * MEAN_AT[0] + MEAN_AT[1] + 1)
                spread_mean(1)

            def take_variance():
                dve.wait_ge(r0_ready, PPS * VAR_AT[0] + VAR_AT[1] + 1)
                fold_variance(1)

            for t in range(STATS_FROM + len(LATE_SETS) * STATS_STEPS, STEPS):
                step(t, 0, before={MEAN_AT: take_mean, (MEAN_AT[0], MEAN_AT[1] + 1): lambda: sum_squares(1),
                                   VAR_AT: take_variance})
            with dve.Fori(STEPS, TOTAL) as t:
                step(t, 1)


def kernel(x):
    import numpy as np
    import concourse.bacc as bacc
    from concourse.bass_utils import run_bass_kernel_spmd

    nc = bacc.Bacc("TRN2", target_bir_lowering=False, num_devices=1)
    x = np.ascontiguousarray(x)
    x_dram = nc.dram_tensor("x", x.shape, F32, kind="ExternalInput").ap()
    out_dram = nc.dram_tensor("out", x.shape, F32, kind="ExternalOutput").ap()
    window_ratio_kernel(nc, x_dram, out_dram)
    r = run_bass_kernel_spmd(nc, [{"x": x}], core_ids=[0])
    return r.results[0]["out"]
```

```python
from contextlib import ExitStack

import concourse.bass as bass
from concourse import mybir

F32 = mybir.dt.float32
ALU = mybir.AluOpType
ACT = mybir.ActivationFunctionType
AX = mybir.AxisListType

BATCH, ROWS, W, C = 2, 128, 128, 192
GROUPS = 32
GC = C // GROUPS
W_WIN, C_WIN = 5, 20
W_LO = W_WIN // 2
C_LO = C_WIN // 2
C_HI = C_WIN - C_LO - 1
EPS = 1e-5
TINY = 1e-26

CA = 128
CB = C - CA
NA = CA + C_LO
B0 = CA - C_HI - 1
NB = C - B0

PAIR = 2
STEP = 8
PPS = STEP // PAIR
STEPS = ROWS // STEP
TOTAL = BATCH * STEPS
PAIRS = STEPS * PPS
PCOLS = PAIR * C
TILES = PCOLS // 128
DUO = 2
RING = 4
AHEAD = ((3,), (4,), (5,), (6,)), ((), (4,), (5,), (6, 7))
NONE = ((), (), (), ())

RAW = 10
SLOTS = RAW + STEPS
HOME = (RAW, 0)
LOADS = 8
LOAD_STEPS = STEPS // LOADS

SUMMED = PPS - 1
PADDED = C_LO + C + C_HI
SUMS = {16: C, 8: C + 8, 4: C + C_WIN - 4, 2: C + C_WIN - 2}

KEEP_WARM = 32

BLOCK = 32
BLOCKS = ROWS // BLOCK
SPB = BLOCK // STEP
LATE_SETS = ((0, 3), (1, 2))
TRIPLES = (2 * BLOCKS, 2 * len(LATE_SETS))
COUNT = tuple(ROWS * GC // n for n in TRIPLES)
ACT_GROUPS = 8
DVE_GROUPS = GROUPS - ACT_GROUPS
ACT_COUNT = ROWS * GC
SET_FROM = (7, RAW)
REST = 12
LEFT = [(j, g) for j in range(len(LATE_SETS)) for g in range(PPS * (REST - SET_FROM[j]), DVE_GROUPS)]
ACT_STEPS = 2 * ACT_GROUPS // PPS
POOL_TO = RAW + ACT_STEPS
MEAN_AT, VAR_AT = (STEPS - 1, 1), (STEPS - 1, 3)
JOIN_AT = (STEPS - 2, 3)


def static(v):
    return isinstance(v, int)


def wait_count(eng, sem, count):
    if not static(count) or count > 0:
        eng.wait_ge(sem, count)


def window_ratio_kernel(nc, x, out):
    ctx = ExitStack()
    with ctx:
        sb = lambda name, shape: ctx.enter_context(nc.sbuf_tensor(name, shape, F32))
        ps = lambda name: ctx.enter_context(nc.psum_tensor(name, [128, 512], F32))
        sem = lambda name: ctx.enter_context(nc.semaphore(name))

        xs = sb("xs", [128, SLOTS * STEP, C])
        xc = sb("xc", [128, RING, PCOLS])
        xc2 = sb("xc2", [128, RING, PCOLS])
        s2 = [sb(f"s2_{i}", [128, PCOLS]) for i in range(2)]
        u = [sb(f"u_{i}", [128, PCOLS]) for i in range(2)]
        q = [sb(f"q_{i}", [128, PCOLS]) for i in range(2)]
        t1 = sb("t1", [128, PPS, PCOLS])
        t2 = sb("t2", [128, DUO, PCOLS])
        b5 = sb("b5", [128, W])
        b5d = sb("b5d", [128, W])
        b20a = sb("b20a", [128, NA])
        b20b = sb("b20b", [128, PAIR, NB])
        b20a_r = [sb(f"b20a_r{b}", [128, NA]) for b in range(BATCH)]
        b20b_r = [sb(f"b20b_r{b}", [128, PAIR, NB]) for b in range(BATCH)]
        mean_c = [sb(f"mean_c{b}", [128, C]) for b in range(BATCH)]
        averager = [sb(f"averager{b}", [128, 128]) for b in range(BATCH)]
        c1_row = sb("c1_row", [128, W])
        c1_mean = sb("c1_mean", [128, PCOLS])
        tiny_bias = sb("tiny_bias", [128, 1])
        wins = sb("wins", [128, 2, PAIR, PADDED])
        padded = wins[:, 0, :, :]
        win2_8 = wins[:, 1, :, :]
        win4 = sb("win4", [128, PAIR, PADDED])
        unused = wins[:, :, :, :].rearrange("p i r c -> p (i r c)")[:, 0:ACT_COUNT]\
            .rearrange("p (r c) -> p r c", c=GC)
        act_sums = sb("act_sums", [128, 2, ACT_GROUPS])
        act_m2 = sb("act_m2", [128, ACT_GROUPS])
        inv_var_g = sb("inv_var_g", [128, GROUPS])
        inv_var_c = sb("inv_var_c", [128, C])
        triples = [sb(f"triples{b}", [128, GROUPS, TRIPLES[b], 3]) for b in range(BATCH)]
        dev = sb("dev", [128, GROUPS, TRIPLES[0]])
        mean_sum = sb("mean_sum", [128, GROUPS])
        dev_sum = sb("dev_sum", [128, GROUPS])
        m2_sum = sb("m2_sum", [128, GROUPS])
        ssq_c = sb("ssq_c", [128, C])
        inv_var = sb("inv_var", [128, 2])

        S = [ps("S0"), ps("S1")]
        U = [ps("U0"), ps("U1")]
        D = [ps("D0"), ps("D1")]
        N = [ps("N0"), ps("N1")]
        mean_ps = D[1][:, PCOLS:PCOLS + GROUPS]
        var_ps = D[1][:, PCOLS + GROUPS:PCOLS + GROUPS + 2]
        var_g_ps = D[1][:, PCOLS + GROUPS + 2:PCOLS + 2 * GROUPS + 2]
        c1_mean_ps = N[1][:, 0:PCOLS]

        loaded0 = [sem(f"loaded0_{j}") for j in range(LOADS)]
        loaded1 = [sem(f"loaded1_{j}") for j in range(len(LATE_SETS))]
        raw_kept = sem("raw_kept")
        c1_mean_in_psum = sem("c1_mean_in_psum")
        c1_mean_ready = sem("c1_mean_ready")
        raw_centred = sem("raw_centred")
        consts_ready = sem("consts_ready")
        pool_own = sem("pool_own")
        dve_own = sem("dve_own")
        mean_sum_ready = sem("mean_sum_ready")
        mean_in_psum = sem("mean_in_psum")
        ssq_ready = sem("ssq_ready")
        var_in_psum = sem("var_in_psum")
        mean_ready = sem("mean_ready")
        b20_ready = sem("b20_ready")
        inv_var_c_ready = sem("inv_var_c_ready")
        scaled = sem("scaled")
        win2_ready = sem("win2_ready")
        win4_ready = sem("win4_ready")
        win_ready = sem("win_ready")
        summed_ready = sem("summed_ready")
        xc_ready = sem("xc_ready")
        xc2_ready = sem("xc2_ready")
        s_ready = sem("s_ready")
        u_ready = sem("u_ready")
        s2_ready = sem("s2_ready")
        us_ready = sem("us_ready")
        d_ready = sem("d_ready")
        n_ready = sem("n_ready")
        r0_ready = sem("r0_ready")
        q_ready = sem("q_ready")
        measured = sem("measured")
        act_measured = sem("act_measured")
        t1_ready = sem("t1_ready")
        t2_ready = sem("t2_ready")
        ratio_ready = sem("ratio_ready")
        out_ready = sem("out_ready")
        stored = [sem("stored0"), sem("stored1")]

        block = ctx.enter_context(nc.Block())

        def is_summed(t, k, b):
            return b == 1 and k == SUMMED and not (static(t) and t == TOTAL - 1)

        def u_count(t, k, b):
            if b == 0:
                return PPS * t + k + 1
            return PAIRS + (PPS - 1) * (t - STEPS) + k + 1 - (k == SUMMED and is_summed(t, k, b))

        def u_count_before(t, k, back, b):
            return u_count(t - (k < back), (k - back) % PPS, b)

        def x_rows(n, b, pairs=1):
            return xs[:, bass.ds((n - b * PAIRS) * PAIR + HOME[b] * STEP, pairs * PAIR), :]

        def dram_rows(t, b, n, pairs):
            return t[b, bass.ds((n - b * PAIRS) * PAIR, pairs * PAIR), :, :].rearrange("h w c -> w h c")

        def raw_box(n, pairs=1):
            flat = xs[:, 0:RAW * STEP, :].rearrange("p r c -> p (r c)")
            return flat[:, bass.ds(n * PCOLS, pairs * PCOLS)]

        @block.sync
        def _(sp):
            for j in range(LOADS):
                sp.dma_start(x_rows(j * LOAD_STEPS * PPS, 0, LOAD_STEPS * PPS),
                             dram_rows(x, 0, j * LOAD_STEPS * PPS, LOAD_STEPS * PPS)).then_inc(loaded0[j], 16)

            def store(t, b, parity):
                sp.wait_ge(out_ready, (PPS // DUO) * (t + 1))
                sp.dma_start(dram_rows(out, b, t * PPS, PPS), x_rows(PPS * t, b, PPS)).then_inc(stored[parity], 16)

            def load1(t):
                arrived = next(loaded1[j] for j, blocks in enumerate(LATE_SETS) if t // SPB in blocks)
                n = PAIRS + PPS * t
                sp.dma_start(x_rows(n, 1, PPS), dram_rows(x, 1, n, PPS)).then_inc(arrived, 16)

            for t in range(STEPS):
                if t < RAW:
                    sp.wait_ge(s2_ready, PPS * (t + 1))
                    load1(t)
                if 0 < t <= STEPS - RAW:
                    sp.wait_ge(stored[(t - 1) % 2], 16 * ((t - 1) // 2 + 1))
                    load1(RAW + t - 1)
                store(t, 0, t % 2)
            with sp.Fori(STEPS // 2, STEPS - 1) as i:
                store(2 * i, 1, 0)
                store(2 * i + 1, 1, 1)
            store(TOTAL - 2, 1, 0)
            for k in range(PPS):
                n = PPS * (TOTAL - 1) + k
                sp.wait_ge(out_ready, (PPS // DUO) * (TOTAL - 1) + k + 1)
                sp.dma_start(dram_rows(out, 1, n, 1), x_rows(n, 1)).then_inc(stored[1], 16)
            sp.wait_ge(stored[0], 16 * TOTAL // 2)
            sp.wait_ge(stored[1], 16 * (TOTAL // 2 - 1 + PPS))

        def wait_loaded1(eng, j):
            eng.wait_ge(loaded1[j], 16 * SPB * len(LATE_SETS[j]))

        @block.gpsimd
        def _(pool):
            own = [0]

            def band(ap, conditions):
                nc.gpsimd.memset(ap, 1.0).then_inc(pool_own, 1)
                own[0] += 1
                for base, channel, pattern in conditions:
                    pool.wait_ge(pool_own, own[0])
                    nc.gpsimd.affine_select(out=ap, in_=ap, compare_op=ALU.is_ge, fill=0.0, base=base,
                                            pattern=pattern, channel_multiplier=channel)\
                      .then_inc(pool_own, 1)
                    own[0] += 1

            band(b5[:, :], [(W_LO, -1, [[1, W]]), (W_LO, 1, [[-1, W]])])
            band(b20a[:, :], [(C_HI, -1, [[1, NA]]), (C_LO, 1, [[-1, NA]])])
            band(b20b[:, :, :], [
                (B0 - CA + C_HI, -1, [[CB, PAIR], [1, NB]]), (CA - B0 + C_LO, 1, [[-CB, PAIR], [-1, NB]]),
                (0, 1, [[-CB, PAIR], [0, NB]]), (CB - 1, -1, [[CB, PAIR], [0, NB]])])
            pool.wait_ge(pool_own, own[0])
            nc.gpsimd.memset(averager[1][:, :], 1.0 / (TRIPLES[1] * 128))
            nc.gpsimd.memset(averager[0][:, :], 1.0 / (TRIPLES[0] * 128)).then_inc(consts_ready, 1)

            def centre_raw(n):
                box = raw_box(n, DUO).rearrange("p (n w) -> p n w", n=DUO)
                nc.gpsimd.tensor_tensor(box, box, c1_mean[:, :].unsqueeze(1).to_broadcast([128, DUO, PCOLS]),
                                        ALU.subtract).then_inc(raw_centred, 1)

            def centre(n, k, b):
                wait_count(pool, s_ready, n - RING + 1)
                wait_count(pool, xc2_ready, n - RING + 1)
                for c0, c1 in ((0, CA), (CA, C)):
                    to = xc[:, k % RING, PAIR * c0:PAIR * c1].rearrange("p (r c) -> p r c", r=PAIR)
                    mean = mean_c[b][:, c0:c1].unsqueeze(1).to_broadcast([128, PAIR, c1 - c0])
                    last = nc.gpsimd.tensor_tensor(to, x_rows(n, b)[:, :, c0:c1], mean, ALU.subtract)
                last.then_inc(xc_ready, 1)

            def square(n, k):
                pool.wait_ge(xc_ready, n + 1)
                pool.wait_ge(xc2_ready, n)
                pool.wait_ge(u_ready, n - RING + 1)
                rows = xc[:, k % RING, :]
                nc.gpsimd.tensor_tensor(xc2[:, k % RING, :], rows, rows, ALU.mult).then_inc(xc2_ready, 1)

            def add_shifted(to, source, shift, n):
                return nc.gpsimd.tensor_tensor(to[:, :, 0:n], source[:, :, 0:n], source[:, :, shift:shift + n],
                                               ALU.add)

            def sum_fours(t):
                i = t - STEPS + 1
                pool.wait_ge(xc2_ready, PPS * t + SUMMED + 1)
                pool.wait_ge(inv_var_c_ready, 1)
                for c0, c1 in ((0, CA), (CA, C)):
                    source = xc2[:, SUMMED, PAIR * c0:PAIR * c1].rearrange("p (r c) -> p r c", r=PAIR)
                    last = nc.gpsimd.tensor_tensor(
                        padded[:, :, C_LO + c0:C_LO + c1], source,
                        inv_var_c[:, c0:c1].unsqueeze(1).to_broadcast([128, PAIR, c1 - c0]), ALU.mult)
                last.then_inc(scaled, 1)
                pool.wait_ge(scaled, i)
                add_shifted(win2_8, padded, 1, SUMS[2]).then_inc(win2_ready, 1)
                pool.wait_ge(win2_ready, i)
                add_shifted(win4, win2_8, 2, SUMS[4]).then_inc(win4_ready, 1)

            def step(t, b, raw=False, squaring=False):
                for k in range(0, PPS, DUO):
                    if raw:
                        centre_raw(PPS * t + k)
                    for m in range(k + DUO, k + 2 * DUO):
                        if b and m == PPS + 1:
                            sum_fours(t)
                        centre(PPS * t + m, m, b)
                        if squaring:
                            square(PPS * t + m, m)

            for j in range(LOADS):
                pool.wait_ge(loaded0[j], 16)
            pool.wait_ge(raw_kept, PPS * RAW)
            pool.wait_ge(mean_ready, 1)
            for n in range(DUO):
                centre(n, n, 0)
            pool.wait_ge(c1_mean_ready, 1)
            step(0, 0, True)
            with pool.Fori(1, RAW) as t:
                step(t, 0, True)
            with pool.Fori(RAW, POOL_TO) as t:
                step(t, 0, squaring=True)
            with pool.Fori(POOL_TO, STEPS - 1) as t:
                step(t, 0)
            for n in (PAIRS - 2, PAIRS - 1):
                centre(n, n, 0)
            for j in range(len(LATE_SETS)):
                wait_loaded1(pool, j)
            pool.wait_ge(act_measured, 2 * ACT_GROUPS)
            nc.gpsimd.memset(padded[:, :, :], 0.0).then_inc(pool_own, 1)
            pool.wait_ge(pool_own, own[0] + 1)
            pool.wait_ge(mean_ready, 2)
            for n in (PAIRS, PAIRS + 1):
                centre(n, n, 1)
            with pool.Fori(STEPS, TOTAL - 1) as t:
                step(t, 1)
            for n in (2 * PAIRS - 2, 2 * PAIRS - 1):
                centre(n, n, 1)

        @block.scalar
        def _(act):
            def square_s(t, k, raw):
                n = PPS * t + k
                if raw:
                    act.wait_ge(raw_centred, (PPS // DUO) * t + k // DUO + 1)
                    source = raw_box(n)
                else:
                    act.wait_ge(s_ready, n + 1)
                    source = S[k % 2][:, 0:PCOLS]
                wait_count(act, n_ready, n - 1)
                nc.scalar.activation(s2[k % 2][:, :], source, ACT.Square).then_inc(s2_ready, 1)

            def keep_u(t, k, b):
                n = PPS * t + k
                act.wait_ge(u_ready, u_count(t, k, b))
                wait_count(act, d_ready, n - 1)
                nc.scalar.activation(u[k % 2][:, :], U[k % 2][:, 0:PCOLS], ACT.Copy).then_inc(us_ready, 1)

            def take_root(n, k):
                act.wait_ge(d_ready, n + 1)
                wait_count(act, t2_ready, n - 1)
                nc.scalar.activation(q[k % 2][:, :], D[k % 2][:, 0:PCOLS], ACT.Abs_reciprocal_sqrt,
                                     bias=tiny_bias[:, 0:1]).then_inc(r0_ready, 1)

            def square_root(n, k):
                act.wait_ge(r0_ready, n + 1)
                nc.scalar.activation(q[k % 2][:, :], q[k % 2][:, :], ACT.Square).then_inc(q_ready, 1)

            def square_xc(t, k, b):
                n = PPS * t + k
                if static(t) and (t, k) == (POOL_TO, 2):
                    act.wait_ge(xc2_ready, n)
                act.wait_ge(xc_ready, n + 1)
                if b and k == SUMMED:
                    act.wait_ge(d_ready, n - RING + 1)
                else:
                    wait_count(act, u_ready, u_count(t - 1, k, b))
                nc.scalar.activation(xc2[:, k % RING, :], xc[:, k % RING, :], ACT.Square).then_inc(xc2_ready, 1)

            def measure(kind, i):
                first, c = HOME[1] * STEP, (DVE_GROUPS + i) * GC
                nc.scalar.activation(unused, xs[:, first:first + ROWS, bass.ds(c, GC)],
                                     (ACT.Identity, ACT.Square)[kind], scale=-1.0, bias=xs[:, first, bass.ds(c, 1)],
                                     accum_out=act_sums[:, kind, bass.ds(i, 1)]).then_inc(act_measured, 1)

            def step(t, b, raw=False, to_raw=False, last=False, ahead=None, measuring=None):
                b_next = 1 if static(t) and t == STEPS - 1 else b
                for k in range(PPS):
                    n = PPS * t + k
                    end = k == PPS - 1
                    if not (last and end):
                        square_s(t + end, (k + 1) % PPS, to_raw if end else raw)
                        if not is_summed(t, k + 1, b):
                            keep_u(t + end, (k + 1) % PPS, b_next if end else b)
                    take_root(n, k)
                    for m in (ahead or AHEAD[b])[k]:
                        square_xc(t + m // PPS, m % PPS, b_next if m >= PPS else b)
                    square_root(n, k)
                    if measuring is not None:
                        measure(measuring, PPS * (t - RAW) + k - measuring * ACT_GROUPS)

            act.wait_ge(consts_ready, 2)
            nc.scalar.activation(q[0][:, 0:1], tiny_bias[:, 0:1], ACT.Abs_reciprocal_sqrt)
            for n in range(PPS * RAW):
                act.wait_ge(s_ready, n + 1)
                nc.scalar.activation(raw_box(n), S[n % 2][:, 0:PCOLS], ACT.Copy).then_inc(raw_kept, 1)
            square_xc(0, 0, 0)
            act.wait_ge(c1_mean_in_psum, 1)
            nc.scalar.activation(c1_mean[:, :], c1_mean_ps, ACT.Copy).then_inc(c1_mean_ready, 1)
            square_xc(0, 1, 0)
            keep_u(0, 0, 0)
            square_s(0, 0, True)
            step(0, 0, True, True, ahead=((2, 3), (4,), (5,), (6,)))
            with act.Fori(1, RAW - 1) as t:
                step(t, 0, True, True)
            step(RAW - 1, 0, True, False, ahead=((3,), (4,), (5,), ()))
            for j in range(len(LATE_SETS)):
                wait_loaded1(act, j)
            with act.Fori(RAW, RAW + ACT_STEPS // 2) as t:
                step(t, 0, ahead=NONE, measuring=0)
            with act.Fori(RAW + ACT_STEPS // 2, POOL_TO - 1) as t:
                step(t, 0, ahead=NONE, measuring=1)
            step(POOL_TO - 1, 0, ahead=((), (), (), (6,)), measuring=1)
            for t in range(POOL_TO, STEPS - 1):
                step(t, 0)
            step(STEPS - 1, 0, ahead=((3,), (), (4,), (5, 6)))
            step(STEPS, 1, ahead=((3,), (4,), (5,), (6, 7)))
            with act.Fori(STEPS + 1, TOTAL - 1) as t:
                step(t, 1)
            step(TOTAL - 1, 1, last=True, ahead=NONE)

        @block.tensor
        def _(pe):
            def box5(bank, data, k, weights):
                for j in range(TILES):
                    tile = data[:, k % RING, 128 * j:128 * (j + 1)]
                    mm = nc.tensor.matmul(bank[k % 2][:, 128 * j:128 * (j + 1)], tile, weights[:, :],
                                          start=True, stop=True)
                return mm

            def box5_raw(n):
                for r in range(PAIR):
                    row, half = HOME[0] * STEP + PAIR * n + r, slice(CB * r, CB * (r + 1))
                    nc.tensor.matmul(S[n % 2][:, 128 * r:128 * (r + 1)], xs[:, row, 0:CA], b5[:, :],
                                     start=True, stop=True)
                    mm = nc.tensor.matmul(S[n % 2][half, 128 * PAIR:PCOLS], xs[:, row, CA:C], b5[:, :],
                                          start=True, stop=True)
                return mm

            def first_stage(t, k, b, raw=False):
                n = PPS * t + k
                if not raw:
                    pe.wait_ge(xc_ready, n + 1)
                    wait_count(pe, s2_ready, n - 1)
                    box5(S, xc, k, b5).then_inc(s_ready, 1)
                if is_summed(t, k, b):
                    return
                pe.wait_ge(xc2_ready, n + 1)
                wait_count(pe, us_ready, u_count_before(t, k, 2, b))
                box5(U, xc2, k, b5d).then_inc(u_ready, 1)

            def box20(bank, data, b):
                o = bank[:, 0:PCOLS].rearrange("p (r c) -> p r c", r=PAIR)
                nc.tensor.matmul(o[:, 0, 0:NA], data[:, 0:128], b20a_r[b][:, :], start=True, stop=False,
                                 skip_group_check=True)
                nc.tensor.matmul(o[:, 1, 0:NA], data[:, 128:256], b20a_r[b][:, :], start=False, stop=False,
                                 skip_group_check=True)
                return nc.tensor.matmul(o[:, :, B0:C], data[:, 256:384], b20b_r[b][:, :, :], start=False, stop=True,
                                        skip_group_check=True)

            def second_stage(t, k, b, extra=None):
                n = PPS * t + k
                wait_count(pe, t1_ready, n - 1)
                if is_summed(t, k, b):
                    pe.wait_ge(summed_ready, t - STEPS + 1)
                    mm = nc.tensor.matmul(D[k % 2][:, 0:PCOLS], b5d[:, :], xc2[:, k, :], start=True, stop=True)
                else:
                    pe.wait_ge(us_ready, u_count(t, k, b))
                    mm = box20(D[k % 2], u[k % 2], b)
                if extra is not None:
                    mm = extra()
                mm.then_inc(d_ready, 1)
                pe.wait_ge(s2_ready, n + 1)
                wait_count(pe, t2_ready, n - 1)
                box20(N[k % 2], s2[k % 2], b).then_inc(n_ready, 1)

            def average_means(b):
                pe.wait_ge(mean_sum_ready, b + 1)
                return nc.tensor.matmul(mean_ps, averager[b][:, :], mean_sum[:, :], start=True, stop=True)

            def average_squares(b):
                pe.wait_ge(ssq_ready, b + 1)
                if b:
                    nc.tensor.matmul(var_g_ps, averager[0][:, :], ssq_c[:, 0:C:GC], start=True, stop=True)
                column = averager[0][:, 0:1]
                nc.tensor.matmul(var_ps[:, 0:1], ssq_c[:, 0:CA], column, start=True, stop=True)
                for r in range(PAIR):
                    mm = nc.tensor.matmul(var_ps[CB * r:CB * (r + 1), 1:2], ssq_c[:, CA:C], column,
                                          start=True, stop=True)
                return mm

            def spread_c1_mean():
                for r in range(PAIR):
                    cols, half = slice(128 * r, 128 * (r + 1)), slice(CB * r, CB * (r + 1))
                    nc.tensor.matmul(c1_mean_ps[:, cols], mean_c[0][0:1, 0:CA], c1_row[0:1, :],
                                     start=True, stop=True)
                    mm = nc.tensor.matmul(c1_mean_ps[half, 128 * PAIR:PCOLS], mean_c[0][0:1, CA:C], c1_row[0:1, :],
                                          start=True, stop=True)
                return mm

            def step(t, b, raw=False, to_raw=False, last=False, begun=False, extras=None):
                b_next = 1 if static(t) and t == STEPS - 1 else b
                for k in range(PPS):
                    end = k == PPS - 1
                    if not (last and end or begun and k == 0):
                        first_stage(t + end, (k + 1) % PPS, b_next if end else b, to_raw if end else raw)
                    second_stage(t, k, b, extras.get((t, k)) if extras else None)

            pe.wait_ge(consts_ready, 2)
            for n in range(PPS * RAW):
                if n % (PPS * LOAD_STEPS) == 0:
                    pe.wait_ge(loaded0[n // (PPS * LOAD_STEPS)], 16)
                wait_count(pe, raw_kept, n - 1)
                box5_raw(n).then_inc(s_ready, 1)
            for _ in range(KEEP_WARM):
                nc.tensor.matmul(N[0][:, 0:W], b5[:, :], b5[:, :], start=True, stop=True)
            average_means(0).then_inc(mean_in_psum, 1)
            pe.wait_ge(mean_ready, 1)
            spread_c1_mean().then_inc(c1_mean_in_psum, 1)
            first_stage(0, 0, 0, True)
            average_squares(0).then_inc(var_in_psum, 1)
            first_stage(0, 1, 0, True)
            pe.wait_ge(c1_mean_ready, 1)
            pe.wait_ge(b20_ready, 1)
            step(0, 0, True, True, begun=True)
            with pe.Fori(1, RAW - 1) as t:
                step(t, 0, True, True)
            pe.wait_ge(raw_kept, PPS * RAW)
            step(RAW - 1, 0, True, False)
            with pe.Fori(RAW, MEAN_AT[0]) as t:
                step(t, 0)
            for t in range(MEAN_AT[0], STEPS):
                step(t, 0, extras={MEAN_AT: lambda: average_means(1), VAR_AT: lambda: average_squares(1)})
            pe.wait_ge(b20_ready, 2)
            with pe.Fori(STEPS, TOTAL - 1) as t:
                step(t, 1)
            step(TOTAL - 1, 1, last=True)

        @block.vector
        def _(dve):
            own = [0]

            def link(ins):
                own[0] += 1
                ins.then_inc(dve_own, 1)
                dve.wait_ge(dve_own, own[0])

            def measure(b, j, g0, count):
                for g in range(count):
                    home = HOME[b] * STEP
                    rows = xs[:, home:home + ROWS, bass.ds((g0 + g) * GC, GC)]\
                        .rearrange("p (a r) c -> p a r c", r=BLOCK)
                    if b:
                        first, second = LATE_SETS[j]
                        rows = rows[:, first:second + 1:second - first, :, :]
                    else:
                        rows = rows[:, j, :, :]
                    to = triples[b][:, bass.ds(g0 + g, 1), 2 * j:2 * j + 2, :]
                    last = nc.vector.bn_stats(to.rearrange("p g a b -> p (g a b)"), rows)
                return last

            def sum_triples(b):
                nc.vector.tensor_reduce(mean_sum[:, :], triples[b][:, :, :, 1], AX.X, ALU.add)\
                  .then_inc(mean_sum_ready, 1)
                nc.vector.tensor_reduce(m2_sum[:, :], triples[b][:, :, :, 2], AX.X, ALU.add)

            def spread_mean(b):
                mean_g = mean_ps.unsqueeze(2)
                nc.vector.tensor_copy(mean_c[b][:, :].rearrange("p (g c) -> p g c", g=GROUPS),
                                      mean_g.to_broadcast([128, GROUPS, GC])).then_inc(mean_ready, 1)
                link(nc.vector.tensor_tensor(dev[:, :, 0:TRIPLES[b]], triples[b][:, :, :, 1],
                                             mean_g.to_broadcast([128, GROUPS, TRIPLES[b]]), ALU.subtract))

            def sum_squares(b):
                d = dev[:, :, 0:TRIPLES[b]]
                by_channel = lambda a: a[:, :].unsqueeze(2).to_broadcast([128, GROUPS, GC])
                link(nc.vector.tensor_tensor(d, d, d, ALU.mult))
                link(nc.vector.tensor_reduce(dev_sum[:, :], d, AX.X, ALU.add))
                nc.vector.scalar_tensor_tensor(ssq_c[:, :].rearrange("p (g c) -> p g c", g=GROUPS),
                                               by_channel(dev_sum), float(COUNT[b]), by_channel(m2_sum),
                                               ALU.mult, ALU.add).then_inc(ssq_ready, 1)

            def fold_variance(b):
                link(nc.vector.tensor_scalar(inv_var[:, :], var_ps, 1.0 / COUNT[0], EPS, ALU.mult, ALU.add))
                link(nc.vector.reciprocal(inv_var[:, :], inv_var[:, :]))
                nc.vector.tensor_scalar(b20a_r[b][:, :], b20a[:, :], inv_var[:, 0:1], None, ALU.mult)
                nc.vector.tensor_scalar(b20b_r[b][:, :, :], b20b[:, :, :], inv_var[:, 1:2], None, ALU.mult)\
                  .then_inc(b20_ready, 1)

            def spread_inverse():
                link(nc.vector.tensor_scalar(inv_var_g[:, :], var_g_ps, 1.0 / COUNT[0], EPS, ALU.mult, ALU.add))
                link(nc.vector.reciprocal(inv_var_g[:, :], inv_var_g[:, :]))
                nc.vector.tensor_copy(inv_var_c[:, :].rearrange("p (g c) -> p g c", g=GROUPS),
                                      inv_var_g[:, :].unsqueeze(2).to_broadcast([128, GROUPS, GC]))\
                  .then_inc(inv_var_c_ready, 1)

            def sum_windows(t):
                done = 2 * (t - STEPS)
                boxed = xc2[:, SUMMED, :].rearrange("p (r c) -> p r c", r=PAIR)
                dve.wait_ge(win4_ready, t - STEPS + 1)
                for i, (to, source, shift) in enumerate(((win2_8, win4, 4), (boxed, win2_8, 8))):
                    n = SUMS[2 * shift]
                    nc.vector.tensor_tensor(to[:, :, 0:n], source[:, :, 0:n], source[:, :, shift:shift + n],
                                            ALU.add).then_inc(win_ready, 1)
                    dve.wait_ge(win_ready, done + i + 1)
                nc.vector.tensor_tensor(boxed, boxed, win4[:, :, 16:SUMS[4]], ALU.add).then_inc(summed_ready, 1)

            def quotient(n, k):
                dve.wait_ge(q_ready, n + 1)
                nc.vector.scalar_tensor_tensor(t1[:, k, :], D[k % 2][:, 0:PCOLS], -TINY, q[k % 2][:, :],
                                               ALU.add, ALU.mult).then_inc(t1_ready, 1)
                dve.wait_ge(n_ready, n + 1)
                nc.vector.scalar_tensor_tensor(t2[:, k % DUO, :], N[k % 2][:, 0:PCOLS], TINY, q[k % 2][:, :],
                                               ALU.add, ALU.mult).then_inc(t2_ready, 1)

            def finish(n, k, b, pairs, count):
                flat = lambda a: a.rearrange("p a b -> p (a b)")
                ratio = flat(t1[:, k:k + pairs, :])
                rows = flat(x_rows(n, b, pairs))
                dve.wait_ge(t2_ready, n + pairs)
                nc.vector.scalar_tensor_tensor(ratio, ratio, 2.0, flat(t2[:, k % DUO:k % DUO + pairs, :]),
                                               ALU.add, ALU.mult).then_inc(ratio_ready, 1)
                dve.wait_ge(ratio_ready, count)
                nc.vector.scalar_tensor_tensor(rows, ratio, 1.0, rows, ALU.min, ALU.add).then_inc(out_ready, 1)

            def step(t, b, before=None, after=None, last=False):
                for k in range(PPS):
                    n = PPS * t + k
                    if before and (t, k) in before:
                        before[t, k]()
                    if k == 1 and is_summed(t, SUMMED, b):
                        sum_windows(t)
                    quotient(n, k)
                    if after:
                        after(k)
                    if last:
                        finish(n, k, b, 1, (PPS // DUO) * t + k + 1)
                    elif k % DUO == DUO - 1:
                        finish(n + 1 - DUO, k + 1 - DUO, b, DUO, (PPS // DUO) * t + k // DUO + 1)

            nc.vector.memset(tiny_bias[:, :], -TINY)
            link(nc.vector.memset(c1_row[:, :], float(W_WIN)))
            for e in range(W_LO):
                for w in (e, W - 1 - e):
                    last = nc.vector.memset(c1_row[:, w:w + 1], float(W_LO + 1 + e))
            link(last)
            dve.wait_ge(consts_ready, 1)
            nc.vector.scalar_tensor_tensor(b5d[:, :], b5[:, :], -1.0, c1_row[:, :], ALU.mult, ALU.mult)\
              .then_inc(consts_ready, 1)

            for j in range(BLOCKS):
                for load in range(j * LOADS // BLOCKS, (j + 1) * LOADS // BLOCKS):
                    dve.wait_ge(loaded0[load], 16)
                last = measure(0, j, 0, GROUPS)
            link(last)
            sum_triples(0)
            dve.wait_ge(mean_in_psum, 1)
            spread_mean(0)
            sum_squares(0)
            dve.wait_ge(var_in_psum, 1)
            fold_variance(0)

            def measure1(j, g):
                measure(1, j, g, 1).then_inc(measured, 1)

            def take_act_sums():
                dve.wait_ge(act_measured, 2 * ACT_GROUPS)
                to = triples[1][:, DVE_GROUPS:GROUPS, :, :]
                by_triple = lambda a: a.unsqueeze(2).to_broadcast([128, ACT_GROUPS, TRIPLES[1]])
                total, squares = act_sums[:, 0, :], act_sums[:, 1, :]
                shift = xs[:, HOME[1] * STEP, DVE_GROUPS * GC:C:GC]
                link(nc.vector.tensor_tensor(act_m2[:, :], total, total, ALU.mult))
                nc.vector.scalar_tensor_tensor(to[:, :, :, 1], by_triple(total), -1.0 / ACT_COUNT, by_triple(shift),
                                               ALU.mult, ALU.add)
                link(nc.vector.scalar_tensor_tensor(act_m2[:, :], act_m2[:, :], -1.0 / ACT_COUNT, squares,
                                                    ALU.mult, ALU.add))
                link(nc.vector.tensor_scalar(to[:, :, :, 2], by_triple(act_m2[:, :]), 1.0 / TRIPLES[1], None,
                                             ALU.mult))

            with dve.Fori(0, SET_FROM[0]) as t:
                step(t, 0)
            wait_loaded1(dve, 0)
            with dve.Fori(SET_FROM[0], SET_FROM[1]) as t:
                step(t, 0, after=lambda k: measure1(0, PPS * (t - SET_FROM[0]) + k))
            wait_loaded1(dve, 1)
            with dve.Fori(SET_FROM[1], REST) as t:
                step(t, 0, after=lambda k: (measure1(0, PPS * (t - SET_FROM[0]) + k),
                                            measure1(1, PPS * (t - SET_FROM[1]) + k)))

            def take_mean():
                dve.wait_ge(r0_ready, PPS * MEAN_AT[0] + MEAN_AT[1] + 1)
                spread_mean(1)

            def take_variance():
                dve.wait_ge(r0_ready, PPS * VAR_AT[0] + VAR_AT[1] + 1)
                fold_variance(1)
                spread_inverse()

            def take_sums():
                take_act_sums()
                dve.wait_ge(measured, len(LATE_SETS) * DVE_GROUPS)
                sum_triples(1)

            def measure_rest(t, k):
                for j, g in LEFT[2 * (PPS * (t - REST) + k):][:2]:
                    measure1(j, g)
                if (t, k) == MEAN_AT:
                    sum_squares(1)

            for t in range(REST, STEPS):
                step(t, 0, before={JOIN_AT: take_sums, MEAN_AT: take_mean, VAR_AT: take_variance},
                     after=lambda k: measure_rest(t, k))
            with dve.Fori(STEPS, TOTAL - 1) as t:
                step(t, 1)
            step(TOTAL - 1, 1, last=True)


def kernel(x):
    import numpy as np
    import concourse.bacc as bacc
    from concourse.bass_utils import run_bass_kernel_spmd

    nc = bacc.Bacc("TRN2", target_bir_lowering=False, num_devices=1)
    x = np.ascontiguousarray(x)
    x_dram = nc.dram_tensor("x", x.shape, F32, kind="ExternalInput").ap()
    out_dram = nc.dram_tensor("out", x.shape, F32, kind="ExternalOutput").ap()
    window_ratio_kernel(nc, x_dram, out_dram)
    r = run_bass_kernel_spmd(nc, [{"x": x}], core_ids=[0])
    return r.results[0]["out"]
```
